# Optimizing a Trainium2 kernel written in Bass

```python
import numpy as np
import jax
import jax.numpy as jnp

def _softmax(x, axis=-1):
    return jax.nn.softmax(x, axis=axis)

def _gelu(x):
    return jax.nn.gelu(x, approximate=True)

def _silu(x):
    return jax.nn.silu(x)

def _sigmoid(x):
    return jax.nn.sigmoid(x)

def _layernorm(x, axis=-1, eps=1e-05):
    m = jnp.mean(x, axis=axis, keepdims=True)
    v = jnp.var(x, axis=axis, keepdims=True)
    return (x - m) / jnp.sqrt(v + eps)

def _scatter_add(tgt, idx, src, axis=0):
    return tgt.at[idx].add(src)

def _segment_sum(src, seg, n):
    return jax.ops.segment_sum(src, seg, n)
kernel_name = 'mk_adj_preln_d2_adj_r2_9d710f'

def setup_inputs(seed: int=0):
    np.random.seed(seed)
    _w = jnp.asarray

    def _rec_inputs():
        import jax
        import jax.numpy as jnp
        _gk = jax.random.key(seed)
        x = -0.0002928 + 1 * jax.random.normal(jax.random.fold_in(_gk, 1), (8192, 256), jnp.float32)
        _a = jax.random.bernoulli(jax.random.fold_in(_gk, 2), 0.00195312, (8192, 8192))
        _a = jnp.logical_or(_a, jnp.eye(8192, dtype=bool))
        _af = _a.astype(jnp.float32)
        _af = _af * jax.random.uniform(jax.random.fold_in(_gk, 3), (8192, 8192), jnp.float32, 0.05, 1)
        adj = _af
        return (x, adj)
    x, adj = _rec_inputs()

    def _L0_gnn_setup():
        import jax, jax.numpy as jnp
        import numpy as np

        def _bin_sign(v):
            return jnp.sign(v)

        def _bin_sign_z(v):
            return jnp.maximum(jnp.sign(v), 0.0)
        key = jax.random.key(seed)
        k1, k2, k3 = jax.random.split(key, 3)
        N, D_IN, D_OUT = (4096, 256, 256)
        x = jax.random.normal(k1, (N, D_IN), dtype=jnp.float32)
        support = jax.random.uniform(k2, (N, N), dtype=jnp.float32)
        weight = jax.random.normal(k3, (D_OUT, D_IN), dtype=jnp.float32)
        return {'x': x, 'support': support, 'weight': weight}
    _L0_gnn_all = _L0_gnn_setup()
    _L0_gnn_in = {k: v for k, v in _L0_gnn_all.items() if k in ('weight',)}
    del _L0_gnn_all

    def _L1_gnn_setup():
        import jax, jax.numpy as jnp
        import numpy as np
        N = 4096
        D = 256
        EPS = 1e-12
        key = jax.random.key(seed)
        k1, k2 = jax.random.split(key)
        cur = jax.random.normal(k1, (N, D), dtype=jnp.float32)
        incidence_m = jax.random.normal(k2, (N, N), dtype=jnp.float32)
        return {'cur': cur, 'incidence_m': incidence_m}
    _L1_gnn_all = _L1_gnn_setup()
    _L1_gnn_in = {k: v for k, v in _L1_gnn_all.items() if k in ()}
    del _L1_gnn_all
    return {'x': x, 'adj': adj, 'L0_gnn_weight': _L0_gnn_in['weight']}

def reference(x, adj, L0_gnn_weight):
    import jax
    import jax.numpy as jnp

    def _L0_gnn_ref(x, support, weight):
        import jax, jax.numpy as jnp
        import numpy as np

        def _bin_sign(v):
            return jnp.sign(v)

        def _bin_sign_z(v):
            return jnp.maximum(jnp.sign(v), 0.0)
        bw = _bin_sign(weight)
        ba = _bin_sign_z(x)
        xw = ba @ bw.T
        out = support @ xw
        return jax.nn.relu(out)

    def _L1_gnn_ref(cur, incidence_m):
        import jax, jax.numpy as jnp
        import numpy as np
        N = 4096
        D = 256
        EPS = 1e-12
        mask = incidence_m > 0
        head = jax.lax.stop_gradient(mask.astype(incidence_m.dtype))
        head = head / jnp.maximum(jnp.sqrt(jnp.sum(head * head, axis=-1, keepdims=True)), EPS)
        inc = incidence_m + head
        edge_fea = inc @ cur
        edge_degree = jnp.sum(inc, axis=-1, keepdims=True)
        return edge_fea / edge_degree
    h = jnp.maximum(_layernorm(x, axis=-1), 0.0)
    x = x + _L0_gnn_ref(h, adj, L0_gnn_weight)
    h = jnp.maximum(_layernorm(x, axis=-1), 0.0)
    x = x + _L1_gnn_ref(h, adj)
    return x

_drawn_inputs = setup_inputs


def setup_inputs(seed=0):
    import zlib

    import numpy as np

    out = dict(_drawn_inputs(seed))
    spreads = {}
    factors = {}
    for name, (base, spread) in spreads.items():
        noise = np.random.default_rng([zlib.crc32(name.encode()), seed]).standard_normal(out[name].shape)
        drawn = base * np.exp(spread * noise) if base else spread * noise
        out[name] = jnp.asarray(drawn.astype(out[name].dtype))
    for name, factor in factors.items():
        out[name] = (out[name] * factor).astype(out[name].dtype)
    return out
```

```python
from contextlib import ExitStack

import concourse.bass as bass
from concourse import mybir

ALU = mybir.AluOpType
ACT = mybir.ActivationFunctionType
F32 = mybir.dt.float32
F32R = mybir.dt.float32r
BF16 = mybir.dt.bfloat16

P = 128
TILES = 4
GW = TILES * P
JB = 2
BATCH = JB * GW
ROUND = 4
JR = ROUND * JB
INCS = 2
LN_EPS = 1e-5
NORM_EPS = 1e-12


def two_layers(nc, x, x_t, adj_p, w_t, out):
    N, D = x.shape
    KD = D // P
    J = N // P
    G = N // GW
    NR = J // JR
    NB = NR * ROUND
    K1 = G * NB
    ROW = 2 * D + 2
    assert D == 2 * P and G % 2 == 0 and NR * JR == J and TILES * D == BATCH

    x1_dram = nc.dram_tensor("x1_scratch", [N, D], F32, kind="Internal").ap()
    hlo_dram = nc.dram_tensor("hlo_scratch", [N, D], F32, kind="Internal").ap()
    norm_dram = nc.dram_tensor("norm_scratch", [1, N], F32, kind="Internal").ap()

    x_v = x.rearrange("(t p) d -> p t d", p=P)
    x1_v = x1_dram.rearrange("(t p) d -> p t d", p=P)
    hlo_v = hlo_dram.rearrange("(t p) d -> p t d", p=P)
    out_v = out.rearrange("(t p) d -> p t d", p=P)
    norm_v = norm_dram.rearrange("a (t p) -> p (a t)", p=P)
    xt_v = x_t.rearrange("(k p) n -> p k n", p=P)
    wt_v = w_t.rearrange("(k p) n -> p k n", p=P)

    with ExitStack() as ctx:
        def sb(name, shape, dt=F32):
            return ctx.enter_context(nc.sbuf_tensor(name, shape, dt))

        def sem(name):
            return ctx.enter_context(nc.semaphore(name))

        feats = sb("feats", [P, J, ROW], F32R)
        adj = sb("adj_ring", [P, ROUND, BATCH])
        hi = sb("hi_ring", [P, ROUND, BATCH], F32R)
        lo = sb("lo_ring", [P, ROUND, BATCH], F32R)
        inc = sb("inc_ring", [P, INCS, BATCH])
        xg = sb("x_group", [P, 2, TILES, D])
        xn = sb("x_normed", [P, TILES, D])
        hlo = sb("h_lo", [P, TILES, D], F32R)
        nrow = sb("norm_row", [P, GW])
        sgn_w = sb("sign_w", [P, KD, D], BF16)
        avg = sb("averaging", [P, P])
        ones = sb("ones", [P, 2], BF16)
        rdeg = sb("inv_degree", [P, J])
        sums = sb("sums", [P, TILES, 3])
        bn6 = sb("bn_parts", [P, TILES, 6])
        mv = sb("mean_var", [P, TILES, 2])
        rt = sb("radicand", [P, 2, TILES])
        sq = sb("root", [P, 2, TILES])
        r0 = sb("inv_root_guess", [P, 2, TILES])
        ra = sb("newton_a", [P, 2, TILES])
        rb = sb("newton_b", [P, 2, TILES])
        rc = sb("newton_c", [P, 2, TILES])
        inv = sb("inv_root", [P, 2, TILES])
        deg = sb("degree", [P, TILES])
        deg2 = sb("degree2", [P, TILES])
        ps = ctx.enter_context(nc.psum_tensor("ps", [P, 8, 512], F32))

        masks = inc[:].rearrange("p s e -> p (s e)").bitcast(BF16).rearrange("p (s e) -> p s e", s=ROUND)
        binary = xn[:].rearrange("p t d -> p (t d)").bitcast(BF16).rearrange("p (s k e) -> p s k e", s=2, k=KD)
        w_raw = nrow[:].rearrange("p (k d) -> p k d", k=KD)

        w_in = sem("w_in")
        xt_in = [sem(f"xt_in{q}") for q in range(2)]
        consts = sem("consts")
        sign_ready = sem("sign_ready")
        mean_ready = sem("mean_ready")
        binary_ready = sem("binary_ready")
        xw_ready = sem("xw_ready")
        xw_stored = sem("xw_stored")
        adj_in = [sem(f"adj_in{s}") for s in range(ROUND)]
        hi_ready = sem("hi_ready")
        lo_ready = sem("lo_ready")
        mask_ready = sem("mask_ready")
        u_ready = sem("u_ready")
        inc_ready = sem("inc_ready")
        parts_free = sem("parts_free")
        acc_free = sem("acc_free")
        x_in = sem("x_in")
        x1_ready = sem("x1_ready")
        x1_stored = sem("x1_stored")
        stats = sem("stats")
        rad_ready = sem("rad_ready")
        root_ready = sem("root_ready")
        inv_ready = sem("inv_ready")
        normed = sem("normed")
        hhi_ready = sem("hhi_ready")
        hlo_ready = sem("hlo_ready")
        hlo_stored = sem("hlo_stored")
        norm_stored = sem("norm_stored")
        hlo_in = sem("hlo_in")
        nrow_in = sem("nrow_in")
        nrow_ready = sem("nrow_ready")
        x1_in = sem("x1_in")
        out_stored = sem("out_stored")

        block = ctx.enter_context(nc.Block())

        def mean_bank(q):
            return ps[:, q, :]

        def xw_banks(q):
            return ps[:, 2 + 2 * q:4 + 2 * q, :]

        def acc1(q, t, a, b):
            return ps[:, 4 * q + t, a:b]

        u_ps = ps[:, 0:2, :]

        def norm_ps(q):
            return ps[:, 2 + q, :]

        def acc2(q, t):
            return ps[:, 4 + 2 * q + t // 2, (t % 2) * D:(t % 2 + 1) * D]

        @block.sync
        def _(sp):
            sp.dma_start(w_raw, wt_v).then_inc(w_in, 16)

            def load_adj(k, slot):
                sp.dma_start(adj[:, slot, :], adj_p[bass.ds(k * P, P), :]).then_inc(adj_in[slot], 16)

            def load_xt(c, q):
                sp.dma_start(inc[:, q, :].rearrange("p (k e) -> p k e", k=KD),
                             xt_v[:, :, bass.ds(c * GW, GW)]).then_inc(xt_in[q], 16)

            load_xt(0, 0)
            load_xt(1, 1)
            for s in range(ROUND):
                load_adj(s, s)
            with sp.Fori(1, G // 2) as i:
                for q in range(2):
                    sp.wait_ge(binary_ready, 2 * i + q - 1)
                    load_xt(2 * i + q, q)

            with sp.Fori(1, G * NR) as n:
                for s in range(ROUND):
                    sp.wait_ge(lo_ready, ROUND * n + s - 3)
                    load_adj(ROUND * n + s, s)

            for s in range(ROUND):
                sp.wait_ge(lo_ready, K1 + s - 3)
                load_adj(s, s)
            sp.wait_ge(parts_free, ROUND + K1)
            for m in range(NR):
                sp.wait_ge(hlo_stored, 16 * (2 * m + 2))
                if m:
                    sp.wait_ge(hlo_in, 16 * m)
                sp.dma_start(feats[:, JR * m:JR * (m + 1), D:2 * D].bitcast(F32),
                             hlo_v[:, JR * m:JR * (m + 1), :]).then_inc(hlo_in, 16)
                if m + 1 < NR:
                    for s in range(ROUND):
                        k = ROUND * (m + 1) + s
                        sp.wait_ge(inc_ready, k - 3)
                        load_adj(k, s)
            with sp.Fori(NR, G * NR) as n:
                for s in range(ROUND):
                    sp.wait_ge(inc_ready, ROUND * n + s - 3)
                    load_adj(ROUND * n + s, s)

        @block.gpsimd
        def _(pool):
            nc.gpsimd.memset(avg[:], 1.0 / D).then_inc(consts, 1)
            nc.gpsimd.memset(ones[:], 1.0).then_inc(consts, 1)
            nc.gpsimd.memset(feats[:, :, 2 * D:ROW].bitcast(F32), 1.0).then_inc(consts, 1)
            nc.gpsimd.memset(deg[:], 0.0).then_inc(parts_free, ROUND)
            nc.gpsimd.memset(deg2[:], 0.0).then_inc(acc_free, 2)

            with pool.Fori(0, G * NR) as n:
                for s in range(ROUND):
                    pool.wait_ge(hi_ready, K1 + ROUND * n + s + 1)
                    nc.gpsimd.tensor_tensor(lo[:, s, :], inc[:, s % INCS, :], hi[:, s, :].bitcast(F32),
                                            ALU.subtract).then_inc(lo_ready, 1)

        @block.scalar
        def _(act):
            act.wait_ge(w_in, 16)
            nc.scalar.activation(sgn_w[:], w_raw, ACT.Sign).then_inc(sign_ready, 1)

            with act.Fori(0, G // 2) as i:
                for q in range(2):
                    act.wait_ge(xw_ready, 2 * i + q + 1)
                    nc.scalar.activation(feats[:, bass.ds((2 * i + q) * TILES, TILES), D:2 * D],
                                         xw_banks(q).rearrange("p b (t d) -> p (b t) d", d=D),
                                         ACT.Copy).then_inc(xw_stored, 1)

            def split1(n):
                for s in range(ROUND):
                    act.wait_ge(adj_in[s], 16 * (n + 1))
                    act.wait_ge(parts_free, ROUND * n + s + 1)
                    nc.scalar.activation(hi[:, s, :], adj[:, s, :], ACT.Copy).then_inc(hi_ready, 1)

            def finish1(g, q, first=False):
                if not first:
                    act.wait_ge(norm_stored, 16 * g)
                    act.wait_ge(hlo_stored, 16 * g)
                act.wait_ge(rad_ready, g + 1)
                nc.scalar.activation(sq[:], rt[:], ACT.Sqrt).then_inc(root_ready, 1)
                act.wait_ge(normed, g + 1)
                nc.scalar.activation(feats[:, bass.ds(g * TILES, TILES), 0:D], xn[:],
                                     ACT.Relu).then_inc(hhi_ready, 1)
                act.wait_ge(x1_ready, g + 1)
                act.dma_start(x1_v[:, bass.ds(g * TILES, TILES), :], xg[:, q, :, :]).then_inc(x1_stored, 16)
                act.wait_ge(inv_ready, g + 1)
                act.dma_start(norm_v[:, bass.ds(g * TILES, TILES)], inv[:, 1, :],
                              allow_slow_non_contiguous=True).then_inc(norm_stored, 16)

            def load_x(g, q):
                act.dma_start(xg[:, q, :, :], x_v[:, bass.ds(g * TILES, TILES), :]).then_inc(x_in, 16)

            def store_h_lo(g):
                act.wait_ge(hlo_ready, g + 1)
                act.dma_start(hlo_v[:, bass.ds(g * TILES, TILES), :],
                              hlo[:].bitcast(F32)).then_inc(hlo_stored, 16)

            def group1(g, q, first=False, last=False):
                with act.Fori(1, NR) as m:
                    split1(g * NR + m)
                if not first:
                    store_h_lo(g - 1)
                if not last:
                    if not first:
                        act.wait_ge(x1_stored, 16 * g)
                        load_x(g + 1, 1 - q)
                    split1((g + 1) * NR)
                finish1(g, q, first)

            load_x(0, 0)
            split1(0)
            act.wait_ge(x_in, 16)
            load_x(1, 1)
            group1(0, 0, first=True)
            with act.Fori(0, G // 2 - 1) as i:
                for q in range(2):
                    group1(2 * i + 1 + q, 1 - q)
            group1(G - 1, 1, last=True)
            store_h_lo(G - 1)

            def load_norms(g):
                act.dma_start(nrow[:], norm_dram[:, bass.ds(g * GW, GW)].broadcast_to([P, GW])
                              ).then_inc(nrow_in, 16)

            def copy_norms(g, q):
                act.wait_ge(nrow_in, 16 * (g + 1))
                nc.scalar.activation(norm_ps(q), nrow[:], ACT.Copy).then_inc(nrow_ready, 1)

            def load_x1(g, q):
                act.dma_start(xg[:, q, :, :], x1_v[:, bass.ds(g * TILES, TILES), :]).then_inc(x1_in, 16)

            act.wait_ge(norm_stored, 16 * G)
            load_norms(0)
            act.wait_ge(x1_stored, 16 * G)
            load_x1(0, 0)
            act.wait_ge(acc_free, 2 + G)
            copy_norms(0, 0)
            act.wait_ge(nrow_ready, 1)
            load_norms(1)

            def split2(n):
                for s in range(ROUND):
                    act.wait_ge(inc_ready, ROUND * n + s + 1)
                    act.wait_ge(parts_free, K1 + ROUND * n + s + 1)
                    nc.scalar.activation(hi[:, s, :], inc[:, s % INCS, :], ACT.Copy).then_inc(hi_ready, 1)

            def group2(g, q, first=False, before_last=False, last=False):
                split2(g * NR)
                if not first:
                    act.wait_ge(acc_free, 2 + G + g)
                    act.dma_start(out_v[:, bass.ds((g - 1) * TILES, TILES), :],
                                  xg[:, 1 - q, :, :]).then_inc(out_stored, 16)
                if not last:
                    copy_norms(g + 1, 1 - q)
                if not (last or before_last):
                    act.wait_ge(nrow_ready, g + 2)
                    load_norms(g + 2)
                with act.Fori(1, NR) as m:
                    split2(g * NR + m)
                if not last:
                    if not first:
                        act.wait_ge(out_stored, 16 * g)
                    load_x1(g + 1, 1 - q)

            group2(0, 0, first=True)
            group2(1, 1)
            with act.Fori(1, G // 2 - 1) as i:
                for q in range(2):
                    group2(2 * i + q, q)
            group2(G - 2, 0, before_last=True)
            group2(G - 1, 1, last=True)
            act.wait_ge(acc_free, 2 + 2 * G)
            act.dma_start(out_v[:, (G - 1) * TILES:G * TILES, :], xg[:, 1, :, :]).then_inc(out_stored, 16)
            act.wait_ge(out_stored, 16 * G)

        @block.vector
        def _(dve):
            def make_binary(c, rounds, q):
                dve.wait_ge(xt_in[q], 16 * rounds)
                dve.wait_ge(mean_ready, c + 1)
                nc.vector.tensor_tensor(binary[:, q, :, :],
                                        inc[:, q, :].rearrange("p (k e) -> p k e", k=KD),
                                        mean_bank(q)[:, None, :].broadcast_to([P, KD, GW]),
                                        ALU.is_gt).then_inc(binary_ready, 1)

            make_binary(0, 1, 0)
            make_binary(1, 1, 1)
            with dve.Fori(1, G // 2) as i:
                for q in range(2):
                    dve.wait_ge(xw_ready, 2 * i + q - 1)
                    make_binary(2 * i + q, i + 1, q)
            dve.wait_ge(binary_ready, G)

            def split1(n):
                for s in range(ROUND):
                    dve.wait_ge(adj_in[s], 16 * (n + 1))
                    dve.wait_ge(parts_free, ROUND * n + s + 1)
                    nc.vector.tensor_scalar(masks[:, s, :], adj[:, s, :], 0.0, None,
                                            ALU.is_gt).then_inc(mask_ready, 1)
                    dve.wait_ge(hi_ready, ROUND * n + s + 1)
                    nc.vector.tensor_tensor(lo[:, s, :], adj[:, s, :], hi[:, s, :].bitcast(F32),
                                            ALU.subtract).then_inc(lo_ready, 1)

            STEPS = 10

            def finish1(g, q):
                done = [0]

                def step(ins):
                    done[0] += 1
                    ins.then_inc(stats, 1)

                def settled():
                    dve.wait_ge(stats, g * STEPS + done[0])

                dve.wait_ge(parts_free, ROUND + (g + 1) * NB)
                dve.wait_ge(x_in, 16 * (g + 1))
                acc = ps[:, 4 * q:4 * q + TILES, :]
                nc.vector.scalar_tensor_tensor(out=xg[:, q, :, :], in0=acc[:, :, 0:D], scalar=0.0,
                                               in1=xg[:, q, :, :], op0=ALU.max,
                                               op1=ALU.add).then_inc(x1_ready, 1)
                nc.vector.tensor_copy(sums[:], acc[:, :, D:D + 3]).then_inc(acc_free, 1)
                dve.wait_ge(x1_ready, g + 1)
                for t in range(TILES):
                    ins = nc.vector.bn_stats(bn6[:, t, :], xg[:, q, t, :])
                step(ins)
                settled()
                dve.wait_ge(acc_free, 2 + g + 1)
                step(nc.vector.tensor_scalar(rt[:, 1, :], sums[:, :, 2], NORM_EPS * NORM_EPS, None, ALU.max))
                for t in range(TILES):
                    ins = nc.vector.bn_aggr(mv[:, t, :], bn6[:, t, :])
                step(ins)
                settled()
                nc.vector.tensor_scalar(rt[:, 0, :], mv[:, :, 1], LN_EPS, None, ALU.add).then_inc(rad_ready, 1)
                dve.wait_ge(root_ready, g + 1)
                step(nc.vector.reciprocal(r0[:], sq[:]))
                settled()
                step(nc.vector.tensor_tensor(ra[:], r0[:], r0[:], ALU.mult))
                settled()
                step(nc.vector.tensor_tensor(rb[:], ra[:], rt[:], ALU.mult))
                settled()
                step(nc.vector.tensor_scalar(rc[:], rb[:], -0.5, 1.5, ALU.mult, ALU.add))
                settled()
                nc.vector.tensor_tensor(inv[:], r0[:], rc[:], ALU.mult).then_inc(inv_ready, 1)
                dve.wait_ge(inv_ready, g + 1)
                step(nc.vector.tensor_tensor(deg[:], sums[:, :, 2], inv[:, 1, :], ALU.mult))
                for t in range(TILES):
                    ins = nc.vector.tensor_scalar(xn[:, t, :], xg[:, q, t, :], mv[:, t, 0:1],
                                                  inv[:, 0, t:t + 1], ALU.subtract, ALU.mult)
                ins.then_inc(normed, 1)
                settled()
                step(nc.vector.tensor_tensor(deg2[:], deg[:], sums[:, :, 0], ALU.add))
                settled()
                step(nc.vector.reciprocal(rdeg[:, bass.ds(g * TILES, TILES)], deg2[:]))
                assert done[0] == STEPS
                dve.wait_ge(hhi_ready, g + 1)
                nc.vector.scalar_tensor_tensor(out=hlo[:], in0=xn[:], scalar=0.0,
                                               in1=feats[:, bass.ds(g * TILES, TILES), 0:D].bitcast(F32),
                                               op0=ALU.max, op1=ALU.subtract).then_inc(hlo_ready, 1)

            def group1(g, q, last=False):
                with dve.Fori(1, NR) as m:
                    split1(g * NR + m)
                if not last:
                    split1((g + 1) * NR)
                finish1(g, q)

            split1(0)
            with dve.Fori(0, G // 2 - 1) as i:
                for q in range(2):
                    group1(2 * i + q, q)
            group1(G - 2, 0)
            group1(G - 1, 1, last=True)

            def make_inc(n, q):
                for s in range(ROUND):
                    dve.wait_ge(adj_in[s], 16 * (G * NR + n + 1))
                    dve.wait_ge(inc_ready, ROUND * n + s)
                    nc.vector.scalar_tensor_tensor(
                        out=u_ps, in0=adj[:, s, :].rearrange("p (j e) -> p j e", j=JB), scalar=0.0,
                        in1=norm_ps(q)[:, None, :].broadcast_to([P, JB, GW]), op0=ALU.is_gt,
                        op1=ALU.mult).then_inc(u_ready, 1)
                    dve.wait_ge(u_ready, ROUND * n + s + 1)
                    dve.wait_ge(lo_ready, K1 + ROUND * n + s + 1 - INCS)
                    nc.vector.tensor_tensor(inc[:, s % INCS, :].rearrange("p (j e) -> p j e", j=JB),
                                            adj[:, s, :].rearrange("p (j e) -> p j e", j=JB), u_ps,
                                            ALU.add).then_inc(inc_ready, 1)

            def finish2(g, q):
                dve.wait_ge(parts_free, ROUND + K1 + (g + 1) * NB)
                dve.wait_ge(x1_in, 16 * (g + 1))
                for t in range(TILES):
                    ins = nc.vector.scalar_tensor_tensor(
                        out=xg[:, q, t, :], in0=acc2(q, t), scalar=rdeg[:, bass.ds(g * TILES + t, 1)],
                        in1=xg[:, q, t, :], op0=ALU.mult, op1=ALU.add)
                ins.then_inc(acc_free, 1)

            def group2(g, q, first=False):
                dve.wait_ge(nrow_ready, g + 1)
                make_inc(g * NR, q)
                if not first:
                    finish2(g - 1, 1 - q)
                with dve.Fori(1, NR) as m:
                    make_inc(g * NR + m, q)

            dve.wait_ge(stats, G * STEPS)
            group2(0, 0, first=True)
            group2(1, 1)
            with dve.Fori(1, G // 2) as i:
                for q in range(2):
                    group2(2 * i + q, q)
            finish2(G - 1, 1)

        @block.tensor
        def _(pe):
            mm = nc.tensor.matmul

            def means(rounds, q):
                pe.wait_ge(xt_in[q], 16 * rounds)
                for k in range(KD):
                    ins = mm(mean_bank(q), avg[:], inc[:, q, k * GW:(k + 1) * GW],
                             start=k == 0, stop=k == KD - 1)
                ins.then_inc(mean_ready, 1)

            def products(c, q):
                pe.wait_ge(binary_ready, c + 1)
                for t in range(TILES):
                    for k in range(KD):
                        ins = mm(xw_banks(q)[:, t // 2, (t % 2) * D:(t % 2 + 1) * D],
                                 binary[:, q, k, t * P:(t + 1) * P], sgn_w[:, k, :],
                                 start=k == 0, stop=k == KD - 1)
                ins.then_inc(xw_ready, 1)

            pe.wait_ge(consts, 3)
            means(1, 0)
            means(1, 1)
            pe.wait_ge(sign_ready, 1)
            for q in range(2):
                products(q, q)
                means(2, q)
            with pe.Fori(1, G // 2 - 1) as i:
                for q in range(2):
                    pe.wait_ge(xw_stored, 2 * i)
                    products(2 * i + q, q)
                    means(i + 2, q)
            pe.wait_ge(xw_stored, G - 2)
            for q in range(2):
                products(G - 2 + q, q)

            pe.wait_ge(xw_stored, G)
            pe.wait_ge(binary_ready, G)

            def round1(g, m, q, opens=False):
                n = g * NR + m
                for s in range(ROUND):
                    pe.wait_ge(hi_ready, ROUND * n + s + 1)
                    for j in range(JB):
                        feat = feats[:, bass.ds(m * JR + s * JB + j, 1), D:ROW]
                        for t in range(TILES):
                            at = j * GW + t * P
                            mm(acc1(q, t, 0, D + 2), hi[:, s, at:at + P], feat,
                               start=opens and s == 0 and j == 0, stop=False, skip_group_check=True)
                    pe.wait_ge(mask_ready, ROUND * n + s + 1)
                    for j in range(JB):
                        for t in range(TILES):
                            at = j * GW + t * P
                            mm(acc1(q, t, D + 2, D + 4), masks[:, s, at:at + P], ones[:],
                               start=False, stop=False, skip_group_check=True)
                    pe.wait_ge(lo_ready, ROUND * n + s + 1)
                    for j in range(JB):
                        feat = feats[:, bass.ds(m * JR + s * JB + j, 1), D:ROW]
                        for t in range(TILES):
                            at = j * GW + t * P
                            ins = mm(acc1(q, t, 0, D + 2), lo[:, s, at:at + P], feat,
                                     start=False, stop=False, skip_group_check=True)
                    ins.then_inc(parts_free, 1)

            with pe.Fori(0, G // 2) as i:
                for q in range(2):
                    pe.wait_ge(acc_free, 2 * i + q + 1)
                    round1(2 * i + q, 0, q, opens=True)
                    with pe.Fori(1, NR) as m:
                        round1(2 * i + q, m, q)

            def round2(g, m, q, opens=False):
                n = g * NR + m
                pe.wait_ge(hhi_ready, 2 * m + 2)
                pe.wait_ge(hlo_in, 16 * (m + 1))
                for s in range(ROUND):
                    pe.wait_ge(hi_ready, K1 + ROUND * n + s + 1)
                    for j in range(JB):
                        tile = m * JR + s * JB + j
                        for t in range(TILES):
                            at = j * GW + t * P
                            for part in range(2):
                                mm(acc2(q, t), hi[:, s, at:at + P],
                                   feats[:, bass.ds(tile, 1), part * D:(part + 1) * D],
                                   start=opens and s == 0 and j == 0 and t % 2 == 0 and part == 0,
                                   stop=False, skip_group_check=True)
                    pe.wait_ge(lo_ready, K1 + ROUND * n + s + 1)
                    for j in range(JB):
                        tile = m * JR + s * JB + j
                        for t in range(TILES):
                            at = j * GW + t * P
                            ins = mm(acc2(q, t), lo[:, s, at:at + P], feats[:, bass.ds(tile, 1), 0:D],
                                     start=False, stop=False, skip_group_check=True)
                    ins.then_inc(parts_free, 1)

            pe.wait_ge(acc_free, 2 + G)
            with pe.Fori(0, G // 2) as i:
                for q in range(2):
                    pe.wait_ge(acc_free, G + 1 + 2 * i + q)
                    round2(2 * i + q, 0, q, opens=True)
                    with pe.Fori(1, NR) as m:
                        round2(2 * i + q, m, q)


def kernel(x, adj, L0_gnn_weight):
    import numpy as np
    import concourse.bacc as bacc
    from concourse.bass_utils import run_bass_kernel_spmd

    x, adj, w = np.asarray(x), np.asarray(adj), np.asarray(L0_gnn_weight)
    N = x.shape[0]
    packed = np.ascontiguousarray(
        adj.reshape(N // GW, GW, N // (JB * P), JB, P).transpose(0, 2, 4, 3, 1)).reshape(-1, BATCH)
    arrays = {"x": np.ascontiguousarray(x), "x_t": np.ascontiguousarray(x.T),
              "adj_packed": packed, "w_t": np.ascontiguousarray(w.T)}
    nc = bacc.Bacc("TRN2", target_bir_lowering=False, num_devices=1)
    aps = [nc.dram_tensor(k, a.shape, mybir.dt.from_np(a.dtype), kind="ExternalInput").ap()
           for k, a in arrays.items()]
    out = nc.dram_tensor("out", x.shape, F32, kind="ExternalOutput").ap()
    two_layers(nc, *aps, out)
    return run_bass_kernel_spmd(nc, [arrays], core_ids=[0]).results[0]["out"]
```

```python
from contextlib import ExitStack

import concourse.bass as bass
from concourse import mybir

ALU = mybir.AluOpType
ACT = mybir.ActivationFunctionType
F32 = mybir.dt.float32
F32R = mybir.dt.float32r
BF16 = mybir.dt.bfloat16

P = 128
TILES = 4
GW = TILES * P
JB = 2
BATCH = JB * GW
ROUND = 4
JR = ROUND * JB
INCS = 2
XTS = 4
LN_EPS = 1e-5
NORM_EPS = 1e-12


def two_layers(nc, x, x_t, adj_p, w_t, out):
    N, D = x.shape
    KD = D // P
    J = N // P
    G = N // GW
    NR = J // JR
    NB = NR * ROUND
    K1 = G * NB
    ROW = 2 * D + 2
    assert D == 2 * P and G % XTS == 0 and NR * JR == J and TILES * D == BATCH

    x1_dram = nc.dram_tensor("x1_scratch", [N, D], F32, kind="Internal").ap()
    hlo_dram = nc.dram_tensor("hlo_scratch", [N, D], F32, kind="Internal").ap()
    norm_dram = nc.dram_tensor("norm_scratch", [1, N], F32, kind="Internal").ap()

    x_v = x.rearrange("(t p) d -> p t d", p=P)
    x1_v = x1_dram.rearrange("(t p) d -> p t d", p=P)
    hlo_v = hlo_dram.rearrange("(t p) d -> p t d", p=P)
    out_v = out.rearrange("(t p) d -> p t d", p=P)
    norm_v = norm_dram.rearrange("a (t p) -> p (a t)", p=P)
    xt_v = x_t.rearrange("(k p) n -> p k n", p=P)
    wt_v = w_t.rearrange("(k p) n -> p k n", p=P)

    with ExitStack() as ctx:
        def sb(name, shape, dt=F32):
            return ctx.enter_context(nc.sbuf_tensor(name, shape, dt))

        def sem(name):
            return ctx.enter_context(nc.semaphore(name))

        feats = sb("feats", [P, J, ROW], F32R)
        adj = sb("adj_ring", [P, ROUND, BATCH])
        hi = sb("hi_ring", [P, ROUND, BATCH], F32R)
        lo = sb("lo_ring", [P, ROUND, BATCH], F32R)
        inc = sb("inc_ring", [P, INCS, BATCH])
        xg = sb("x_group", [P, 2, TILES, D])
        h = sb("h_group", [P, TILES, D])
        hlo = sb("h_lo", [P, TILES, D], F32R)
        nrow = sb("norm_row", [P, GW])
        sgn_w = sb("sign_w", [P, KD, D], BF16)
        avg = sb("averaging", [P, P])
        ones = sb("ones", [P, 2], BF16)
        rdeg = sb("inv_degree", [P, J])
        sums = sb("sums", [P, TILES, 3])
        bn6 = sb("bn_parts", [P, TILES, 6])
        mv = sb("mean_var", [P, TILES, 2])
        rt = sb("radicand", [P, 2, TILES])
        sq = sb("root", [P, 2, TILES])
        r0 = sb("inv_root_guess", [P, 2, TILES])
        ra = sb("newton_a", [P, 2, TILES])
        rb = sb("newton_b", [P, 2, TILES])
        rc = sb("newton_c", [P, 2, TILES])
        inv = sb("inv_root", [P, 2, TILES])
        shift = sb("ln_shift", [P, TILES])
        deg = sb("degree", [P, TILES])
        deg2 = sb("degree2", [P, TILES])
        ps = ctx.enter_context(nc.psum_tensor("ps", [P, 8, 512], F32))

        masks = inc[:].rearrange("p s e -> p (s e)").bitcast(BF16).rearrange("p (s e) -> p s e", s=ROUND)
        binary = h[:].rearrange("p t d -> p (t d)").bitcast(BF16).rearrange("p (s k e) -> p s k e", s=2, k=KD)
        xt_buf = [inc[:, 0, :], inc[:, 1, :]] + [xg[:, q, :, :].rearrange("p t d -> p (t d)") for q in range(2)]
        w_raw = nrow[:].rearrange("p (k d) -> p k d", k=KD)

        w_in = sem("w_in")
        xt_in = [sem(f"xt_in{q}") for q in range(XTS)]
        consts = sem("consts")
        sign_ready = sem("sign_ready")
        mean_ready = sem("mean_ready")
        binary_ready = sem("binary_ready")
        xw_ready = sem("xw_ready")
        xw_stored = sem("xw_stored")
        adj_in = [sem(f"adj_in{s}") for s in range(ROUND)]
        hi_ready = sem("hi_ready")
        lo_ready = sem("lo_ready")
        mask_ready = sem("mask_ready")
        u_ready = sem("u_ready")
        inc_ready = sem("inc_ready")
        parts_free = sem("parts_free")
        acc_free = sem("acc_free")
        x_in = sem("x_in")
        x1_ready = sem("x1_ready")
        x1_stored = sem("x1_stored")
        stats = sem("stats")
        rad_ready = sem("rad_ready")
        root_ready = sem("root_ready")
        inv_ready = sem("inv_ready")
        shift_ready = sem("shift_ready")
        h_ready = sem("h_ready")
        hhi_ready = sem("hhi_ready")
        hlo_ready = sem("hlo_ready")
        hlo_stored = sem("hlo_stored")
        norm_stored = sem("norm_stored")
        hlo_in = sem("hlo_in")
        nrow_in = sem("nrow_in")
        nrow_ready = sem("nrow_ready")
        x1_in = sem("x1_in")
        out_stored = sem("out_stored")

        block = ctx.enter_context(nc.Block())

        def mean_bank(q):
            return ps[:, q, :]

        def xw_banks(q):
            return ps[:, 2 + 2 * q:4 + 2 * q, :]

        def acc1(q, t, a, b):
            return ps[:, 4 * q + t, a:b]

        u_ps = ps[:, 0:2, :]

        def norm_ps(q):
            return ps[:, 2 + q, :]

        def acc2(q, t):
            return ps[:, 4 + 2 * q + t // 2, (t % 2) * D:(t % 2 + 1) * D]

        @block.sync
        def _(sp):
            sp.dma_start(w_raw, wt_v).then_inc(w_in, 16)

            def load_adj(k, slot):
                sp.dma_start(adj[:, slot, :], adj_p[bass.ds(k * P, P), :]).then_inc(adj_in[slot], 16)

            def load_xt(c, q):
                sp.dma_start(xt_buf[q].rearrange("p (k e) -> p k e", k=KD),
                             xt_v[:, :, bass.ds(c * GW, GW)]).then_inc(xt_in[q], 16)

            for q in range(XTS):
                load_xt(q, q)
            for s in range(ROUND):
                load_adj(s, s)
            with sp.Fori(1, G // XTS) as i:
                for q in range(XTS):
                    sp.wait_ge(binary_ready, XTS * (i - 1) + q + 1)
                    load_xt(XTS * i + q, q)

            with sp.Fori(1, G * NR) as n:
                for s in range(ROUND):
                    sp.wait_ge(lo_ready, ROUND * n + s - 3)
                    load_adj(ROUND * n + s, s)

            for s in range(ROUND):
                sp.wait_ge(lo_ready, K1 + s - 3)
                load_adj(s, s)
            sp.wait_ge(parts_free, ROUND + K1)
            for m in range(NR):
                sp.wait_ge(hlo_stored, 16 * (2 * m + 2))
                if m:
                    sp.wait_ge(hlo_in, 16 * m)
                sp.dma_start(feats[:, JR * m:JR * (m + 1), D:2 * D].bitcast(F32),
                             hlo_v[:, JR * m:JR * (m + 1), :]).then_inc(hlo_in, 16)
                if m + 1 < NR:
                    for s in range(ROUND):
                        k = ROUND * (m + 1) + s
                        sp.wait_ge(inc_ready, JB * (k - 3))
                        load_adj(k, s)
            with sp.Fori(NR, G * NR) as n:
                for s in range(ROUND):
                    sp.wait_ge(inc_ready, JB * (ROUND * n + s - 3))
                    load_adj(ROUND * n + s, s)

        @block.gpsimd
        def _(pool):
            nc.gpsimd.memset(avg[:], 1.0 / D).then_inc(consts, 1)
            nc.gpsimd.memset(ones[:], 1.0).then_inc(consts, 1)
            nc.gpsimd.memset(feats[:, :, 2 * D:ROW].bitcast(F32), 1.0).then_inc(consts, 1)
            nc.gpsimd.memset(deg[:], 0.0).then_inc(parts_free, ROUND)
            nc.gpsimd.memset(deg2[:], 0.0).then_inc(acc_free, 2)

            with pool.Fori(0, G * NR) as n:
                for s in range(ROUND):
                    pool.wait_ge(hi_ready, K1 + ROUND * n + s + 1)
                    nc.gpsimd.tensor_tensor(lo[:, s, :], inc[:, s % INCS, :], hi[:, s, :].bitcast(F32),
                                            ALU.subtract).then_inc(lo_ready, 1)

        @block.scalar
        def _(act):
            act.wait_ge(w_in, 16)
            nc.scalar.activation(sgn_w[:], w_raw, ACT.Sign).then_inc(sign_ready, 1)

            with act.Fori(0, G // 2) as i:
                for q in range(2):
                    act.wait_ge(xw_ready, 2 * i + q + 1)
                    nc.scalar.activation(feats[:, bass.ds((2 * i + q) * TILES, TILES), D:2 * D],
                                         xw_banks(q).rearrange("p b (t d) -> p (b t) d", d=D),
                                         ACT.Copy).then_inc(xw_stored, 1)

            def split1(n, batches=range(ROUND)):
                for s in batches:
                    act.wait_ge(adj_in[s], 16 * (n + 1))
                    act.wait_ge(parts_free, ROUND * n + s + 1)
                    nc.scalar.activation(hi[:, s, :], adj[:, s, :], ACT.Copy).then_inc(hi_ready, 1)

            def take_roots(g, first=False):
                if not first:
                    act.wait_ge(norm_stored, 16 * g)
                    act.wait_ge(hlo_stored, 16 * g)
                act.wait_ge(rad_ready, g + 1)
                nc.scalar.activation(sq[:], rt[:], ACT.Sqrt).then_inc(root_ready, 1)

            def take_h(g, q, t):
                act.wait_ge(shift_ready, g + 1)
                nc.scalar.activation(h[:, t, :], xg[:, q, t, :], ACT.Relu, bias=shift[:, t:t + 1],
                                     scale=inv[:, 0, t:t + 1]).then_inc(h_ready, 1)

            def h_high(g, q):
                act.wait_ge(h_ready, TILES * (g + 1))
                nc.scalar.activation(feats[:, bass.ds(g * TILES, TILES), 0:D], h[:],
                                     ACT.Copy).then_inc(hhi_ready, 1)
                act.wait_ge(x1_ready, g + 1)
                act.dma_start(x1_v[:, bass.ds(g * TILES, TILES), :], xg[:, q, :, :]).then_inc(x1_stored, 16)
                act.wait_ge(inv_ready, g + 1)
                act.dma_start(norm_v[:, bass.ds(g * TILES, TILES)], inv[:, 1, :],
                              allow_slow_non_contiguous=True).then_inc(norm_stored, 16)

            def load_x(g, q):
                act.dma_start(xg[:, q, :, :], x_v[:, bass.ds(g * TILES, TILES), :]).then_inc(x_in, 16)

            def store_h_lo(g):
                act.wait_ge(hlo_ready, g + 1)
                act.dma_start(hlo_v[:, bass.ds(g * TILES, TILES), :],
                              hlo[:].bitcast(F32)).then_inc(hlo_stored, 16)

            def group1(g, q, first=False, second=False, last=False):
                split1(g * NR + 1)
                if not first:
                    take_roots(g - 1, second)
                split1(g * NR + 2)
                for s in range(ROUND):
                    split1(g * NR + 3, (s,))
                    if not first:
                        take_h(g - 1, 1 - q, s)
                if not first:
                    h_high(g - 1, 1 - q)
                with act.Fori(4, NR) as m:
                    split1(g * NR + m)
                if not first:
                    store_h_lo(g - 1)
                    act.wait_ge(x1_stored, 16 * g)
                    if not last:
                        load_x(g + 1, 1 - q)
                if not last:
                    split1((g + 1) * NR)

            def load_norms(g):
                act.dma_start(nrow[:], norm_dram[:, bass.ds(g * GW, GW)].broadcast_to([P, GW])
                              ).then_inc(nrow_in, 16)

            def copy_norms(g, q):
                act.wait_ge(nrow_in, 16 * (g + 1))
                nc.scalar.activation(norm_ps(q), nrow[:], ACT.Copy).then_inc(nrow_ready, 1)

            def load_x1(g, q):
                act.dma_start(xg[:, q, :, :], x1_v[:, bass.ds(g * TILES, TILES), :]).then_inc(x1_in, 16)

            load_x(0, 0)
            split1(0)
            act.wait_ge(x_in, 16)
            load_x(1, 1)
            group1(0, 0, first=True)
            group1(1, 1, second=True)
            with act.Fori(1, G // 2 - 1) as i:
                for q in range(2):
                    group1(2 * i + q, q)
            group1(G - 2, 0)
            act.wait_ge(norm_stored, 16 * (G - 2))
            load_norms(0)
            group1(G - 1, 1, last=True)
            load_x1(0, 0)
            act.wait_ge(acc_free, 2 + G - 1)
            copy_norms(0, 0)
            act.wait_ge(nrow_ready, 1)
            load_norms(1)

            def split2(n, batches=range(ROUND)):
                for s in batches:
                    act.wait_ge(inc_ready, JB * (ROUND * n + s + 1))
                    act.wait_ge(parts_free, K1 + ROUND * n + s + 1)
                    nc.scalar.activation(hi[:, s, :], inc[:, s % INCS, :], ACT.Copy).then_inc(hi_ready, 1)

            def group2(g, q, first=False, before_last=False, last=False):
                split2(g * NR)
                if first:
                    take_roots(G - 1)
                    split2(1)
                    for s in range(ROUND):
                        split2(2, (s,))
                        take_h(G - 1, 1, s)
                    h_high(G - 1, 1)
                    split2(3)
                    store_h_lo(G - 1)
                    act.wait_ge(norm_stored, 16 * G)
                if not first:
                    act.wait_ge(acc_free, 2 + G + g)
                    act.dma_start(out_v[:, bass.ds((g - 1) * TILES, TILES), :],
                                  xg[:, 1 - q, :, :]).then_inc(out_stored, 16)
                if not last:
                    copy_norms(g + 1, 1 - q)
                if not (last or before_last):
                    act.wait_ge(nrow_ready, g + 2)
                    load_norms(g + 2)
                with act.Fori(4 if first else 1, NR) as m:
                    split2(g * NR + m)
                if not last:
                    if first:
                        act.wait_ge(x1_stored, 16 * G)
                    else:
                        act.wait_ge(out_stored, 16 * g)
                    load_x1(g + 1, 1 - q)

            group2(0, 0, first=True)
            group2(1, 1)
            with act.Fori(1, G // 2 - 1) as i:
                for q in range(2):
                    group2(2 * i + q, q)
            group2(G - 2, 0, before_last=True)
            group2(G - 1, 1, last=True)
            act.wait_ge(acc_free, 2 + 2 * G)
            act.dma_start(out_v[:, (G - 1) * TILES:G * TILES, :], xg[:, 1, :, :]).then_inc(out_stored, 16)
            act.wait_ge(out_stored, 16 * G)

        @block.vector
        def _(dve):
            def make_binary(c, rounds, q):
                dve.wait_ge(xt_in[q], 16 * rounds)
                dve.wait_ge(mean_ready, c + 1)
                if not isinstance(c, int) or c >= 2:
                    dve.wait_ge(xw_ready, c - 1)
                nc.vector.tensor_tensor(binary[:, q % 2, :, :],
                                        xt_buf[q].rearrange("p (k e) -> p k e", k=KD),
                                        mean_bank(q % 2)[:, None, :].broadcast_to([P, KD, GW]),
                                        ALU.is_gt).then_inc(binary_ready, 1)

            for q in range(XTS):
                make_binary(q, 1, q)
            with dve.Fori(1, G // XTS) as i:
                for q in range(XTS):
                    make_binary(XTS * i + q, i + 1, q)
            dve.wait_ge(binary_ready, G)

            def split1(n, **after):
                for s in range(ROUND):
                    dve.wait_ge(adj_in[s], 16 * (n + 1))
                    dve.wait_ge(parts_free, ROUND * n + s + 2 - s % 2)
                    nc.vector.tensor_scalar(masks[:, s, :], adj[:, s, :], 0.0, None,
                                            ALU.is_gt).then_inc(mask_ready, 1)
                    dve.wait_ge(hi_ready, ROUND * n + s + 1)
                    nc.vector.tensor_tensor(lo[:, s, :], adj[:, s, :], hi[:, s, :].bitcast(F32),
                                            ALU.subtract).then_inc(lo_ready, 1)
                    if f"after_{s}" in after:
                        after[f"after_{s}"]()

            STEPS = 10

            def step(ins):
                ins.then_inc(stats, 1)

            def sum_up(g, q):
                dve.wait_ge(parts_free, ROUND + (g + 1) * NB)
                dve.wait_ge(x_in, 16 * (g + 1))
                acc = ps[:, 4 * q:4 * q + TILES, :]
                nc.vector.scalar_tensor_tensor(out=xg[:, q, :, :], in0=acc[:, :, 0:D], scalar=0.0,
                                               in1=xg[:, q, :, :], op0=ALU.max,
                                               op1=ALU.add).then_inc(x1_ready, 1)
                nc.vector.tensor_copy(sums[:], acc[:, :, D:D + 3]).then_inc(acc_free, 1)

            def take_stats(g, q):
                dve.wait_ge(x1_ready, g + 1)
                for t in range(TILES):
                    ins = nc.vector.bn_stats(bn6[:, t, :], xg[:, q, t, :])
                step(ins)

            def take_radicands(g):
                dve.wait_ge(acc_free, 2 + g + 1)
                dve.wait_ge(stats, g * STEPS + 1)
                step(nc.vector.tensor_scalar(rt[:, 1, :], sums[:, :, 2], NORM_EPS * NORM_EPS, None,
                                             ALU.max))
                for t in range(TILES):
                    ins = nc.vector.bn_aggr(mv[:, t, :], bn6[:, t, :])
                step(ins)
                dve.wait_ge(stats, g * STEPS + 3)
                nc.vector.tensor_scalar(rt[:, 0, :], mv[:, :, 1], LN_EPS, None, ALU.add).then_inc(rad_ready, 1)

            def invert_roots(g):
                dve.wait_ge(root_ready, g + 1)
                step(nc.vector.reciprocal(r0[:], sq[:]))
                dve.wait_ge(stats, g * STEPS + 4)
                step(nc.vector.tensor_tensor(ra[:], r0[:], r0[:], ALU.mult))
                dve.wait_ge(stats, g * STEPS + 5)
                step(nc.vector.tensor_tensor(rb[:], ra[:], rt[:], ALU.mult))
                dve.wait_ge(stats, g * STEPS + 6)
                step(nc.vector.tensor_scalar(rc[:], rb[:], -0.5, 1.5, ALU.mult, ALU.add))
                dve.wait_ge(stats, g * STEPS + 7)
                nc.vector.tensor_tensor(inv[:], r0[:], rc[:], ALU.mult).then_inc(inv_ready, 1)

            def take_degree(g):
                dve.wait_ge(inv_ready, g + 1)
                nc.vector.scalar_tensor_tensor(out=shift[:], in0=mv[:, :, 0], scalar=-1.0, in1=inv[:, 0, :],
                                               op0=ALU.mult, op1=ALU.mult).then_inc(shift_ready, 1)
                step(nc.vector.tensor_tensor(deg[:], sums[:, :, 2], inv[:, 1, :], ALU.mult))
                dve.wait_ge(stats, g * STEPS + 8)
                step(nc.vector.tensor_tensor(deg2[:], deg[:], sums[:, :, 0], ALU.add))
                dve.wait_ge(stats, g * STEPS + 9)
                step(nc.vector.reciprocal(rdeg[:, bass.ds(g * TILES, TILES)], deg2[:]))

            def h_low(g):
                dve.wait_ge(hhi_ready, g + 1)
                nc.vector.tensor_tensor(hlo[:], h[:],
                                        feats[:, bass.ds(g * TILES, TILES), 0:D].bitcast(F32),
                                        ALU.subtract).then_inc(hlo_ready, 1)

            def group1(g, q, first=False, last=False):
                c, cq = g - 1, 1 - q
                if first:
                    for m in (1, 2, 3):
                        split1(m)
                else:
                    n = g * NR
                    split1(n + 1, after_0=lambda: take_stats(c, cq), after_1=lambda: take_radicands(c))
                    split1(n + 2, after_0=lambda: invert_roots(c), after_1=lambda: take_degree(c))
                    split1(n + 3)
                split1(g * NR + 4, **({} if first else {"after_0": lambda: h_low(c)}))
                with dve.Fori(5, NR) as m:
                    split1(g * NR + m)
                if not last:
                    split1((g + 1) * NR, after_3=lambda: sum_up(g, q))

            split1(0)
            group1(0, 0, first=True)
            with dve.Fori(0, G // 2 - 1) as i:
                for q in range(2):
                    group1(2 * i + 1 + q, 1 - q)
            group1(G - 1, 1, last=True)

            def make_inc(n, q, **after):
                for s in range(ROUND):
                    k = ROUND * n + s
                    tiles = [slice(j * GW, (j + 1) * GW) for j in range(JB)]
                    dve.wait_ge(adj_in[s], 16 * (G * NR + n + 1))
                    for j in range(JB):
                        if not isinstance(n, int) or n + s:
                            dve.wait_ge(inc_ready, JB * (k - 1) + j + 1)
                        nc.vector.scalar_tensor_tensor(
                            out=u_ps[:, j, :], in0=adj[:, s, tiles[j]], scalar=0.0, in1=norm_ps(q),
                            op0=ALU.is_gt, op1=ALU.mult).then_inc(u_ready, 1)
                    dve.wait_ge(lo_ready, K1 + k + 1 - INCS)
                    for j in range(JB):
                        dve.wait_ge(u_ready, JB * k + j + 1)
                        nc.vector.tensor_tensor(inc[:, s % INCS, tiles[j]], adj[:, s, tiles[j]],
                                                u_ps[:, j, :], ALU.add).then_inc(inc_ready, 1)
                    if f"after_{s}" in after:
                        after[f"after_{s}"]()

            def finish2(g, q):
                dve.wait_ge(parts_free, ROUND + K1 + (g + 1) * NB)
                dve.wait_ge(x1_in, 16 * (g + 1))
                for t in range(TILES):
                    ins = nc.vector.scalar_tensor_tensor(
                        out=xg[:, q, t, :], in0=acc2(q, t), scalar=rdeg[:, bass.ds(g * TILES + t, 1)],
                        in1=xg[:, q, t, :], op0=ALU.mult, op1=ALU.add)
                ins.then_inc(acc_free, 1)

            def group2(g, q):
                dve.wait_ge(nrow_ready, g + 1)
                make_inc(g * NR, q)
                finish2(g - 1, 1 - q)
                with dve.Fori(1, NR) as m:
                    make_inc(g * NR + m, q)

            sum_up(G - 1, 1)
            dve.wait_ge(nrow_ready, 1)
            make_inc(0, 0, after_1=lambda: take_stats(G - 1, 1), after_3=lambda: take_radicands(G - 1))
            make_inc(1, 0, after_1=lambda: invert_roots(G - 1), after_2=lambda: take_degree(G - 1))
            make_inc(2, 0)
            make_inc(3, 0, after_0=lambda: h_low(G - 1))
            with dve.Fori(4, NR) as m:
                make_inc(m, 0)
            dve.wait_ge(stats, G * STEPS)
            group2(1, 1)
            with dve.Fori(1, G // 2) as i:
                for q in range(2):
                    group2(2 * i + q, q)
            finish2(G - 1, 1)

        @block.tensor
        def _(pe):
            mm = nc.tensor.matmul

            def means(rounds, q):
                pe.wait_ge(xt_in[q], 16 * rounds)
                for k in range(KD):
                    ins = mm(mean_bank(q % 2), avg[:], xt_buf[q][:, k * GW:(k + 1) * GW],
                             start=k == 0, stop=k == KD - 1)
                ins.then_inc(mean_ready, 1)

            def products(c, q):
                pe.wait_ge(binary_ready, c + 1)
                if not isinstance(c, int) or c >= 2:
                    pe.wait_ge(xw_stored, c - 1)
                for t in range(TILES):
                    for k in range(KD):
                        ins = mm(xw_banks(q % 2)[:, t // 2, (t % 2) * D:(t % 2 + 1) * D],
                                 binary[:, q % 2, k, t * P:(t + 1) * P], sgn_w[:, k, :],
                                 start=k == 0, stop=k == KD - 1)
                ins.then_inc(xw_ready, 1)

            pe.wait_ge(consts, 3)
            means(1, 0)
            means(1, 1)
            pe.wait_ge(sign_ready, 1)
            for q in range(XTS):
                products(q, q)
                means(1 + (q + 2) // XTS, (q + 2) % XTS)
            with pe.Fori(1, G // XTS - 1) as i:
                for q in range(XTS):
                    products(XTS * i + q, q)
                    means(i + 1 + (q + 2) // XTS, (q + 2) % XTS)
            for q in range(XTS):
                products(G - XTS + q, q)
                if q < 2:
                    means(G // XTS, q + 2)

            pe.wait_ge(xw_stored, G)
            pe.wait_ge(binary_ready, G)

            def round1(g, m, q, opens=False):
                n = g * NR + m
                for s in range(ROUND):
                    pe.wait_ge(hi_ready, ROUND * n + s + 1)
                    for j in range(JB):
                        feat = feats[:, bass.ds(m * JR + s * JB + j, 1), D:ROW]
                        for t in range(TILES):
                            at = j * GW + t * P
                            mm(acc1(q, t, 0, D + 2), hi[:, s, at:at + P], feat,
                               start=opens and s == 0 and j == 0, stop=False, skip_group_check=True)
                    if s % 2:
                        pe.wait_ge(mask_ready, ROUND * n + s + 1)
                        for b in (s - 1, s):
                            for t in range(JB * TILES):
                                mm(acc1(q, t % TILES, D + 2, D + 4), masks[:, b, t * P:(t + 1) * P],
                                   ones[:], start=False, stop=False, skip_group_check=True)
                    pe.wait_ge(lo_ready, ROUND * n + s + 1)
                    for j in range(JB):
                        feat = feats[:, bass.ds(m * JR + s * JB + j, 1), D:ROW]
                        for t in range(TILES):
                            at = j * GW + t * P
                            ins = mm(acc1(q, t, 0, D + 2), lo[:, s, at:at + P], feat,
                                     start=False, stop=False, skip_group_check=True)
                    ins.then_inc(parts_free, 1)

            with pe.Fori(0, G // 2) as i:
                for q in range(2):
                    pe.wait_ge(acc_free, 2 * i + q + 1)
                    round1(2 * i + q, 0, q, opens=True)
                    with pe.Fori(1, NR) as m:
                        round1(2 * i + q, m, q)

            def round2(g, m, q, opens=False):
                n = g * NR + m
                pe.wait_ge(hhi_ready, 2 * m + 2)
                pe.wait_ge(hlo_in, 16 * (m + 1))
                for s in range(ROUND):
                    pe.wait_ge(hi_ready, K1 + ROUND * n + s + 1)
                    for j in range(JB):
                        tile = m * JR + s * JB + j
                        for t in range(TILES):
                            at = j * GW + t * P
                            for part in range(2):
                                mm(acc2(q, t), hi[:, s, at:at + P],
                                   feats[:, bass.ds(tile, 1), part * D:(part + 1) * D],
                                   start=opens and s == 0 and j == 0 and t % 2 == 0 and part == 0,
                                   stop=False, skip_group_check=True)
                    pe.wait_ge(lo_ready, K1 + ROUND * n + s + 1)
                    for j in range(JB):
                        tile = m * JR + s * JB + j
                        for t in range(TILES):
                            at = j * GW + t * P
                            ins = mm(acc2(q, t), lo[:, s, at:at + P], feats[:, bass.ds(tile, 1), 0:D],
                                     start=False, stop=False, skip_group_check=True)
                    ins.then_inc(parts_free, 1)

            pe.wait_ge(acc_free, 2 + G)
            with pe.Fori(0, G // 2) as i:
                for q in range(2):
                    pe.wait_ge(acc_free, G + 1 + 2 * i + q)
                    round2(2 * i + q, 0, q, opens=True)
                    with pe.Fori(1, NR) as m:
                        round2(2 * i + q, m, q)


def kernel(x, adj, L0_gnn_weight):
    import numpy as np
    import concourse.bacc as bacc
    from concourse.bass_utils import run_bass_kernel_spmd

    x, adj, w = np.asarray(x), np.asarray(adj), np.asarray(L0_gnn_weight)
    N = x.shape[0]
    packed = np.ascontiguousarray(
        adj.reshape(N // GW, GW, N // (JB * P), JB, P).transpose(0, 2, 4, 3, 1)).reshape(-1, BATCH)
    arrays = {"x": np.ascontiguousarray(x), "x_t": np.ascontiguousarray(x.T),
              "adj_packed": packed, "w_t": np.ascontiguousarray(w.T)}
    nc = bacc.Bacc("TRN2", target_bir_lowering=False, num_devices=1)
    aps = [nc.dram_tensor(k, a.shape, mybir.dt.from_np(a.dtype), kind="ExternalInput").ap()
           for k, a in arrays.items()]
    out = nc.dram_tensor("out", x.shape, F32, kind="ExternalOutput").ap()
    two_layers(nc, *aps, out)
    return run_bass_kernel_spmd(nc, [arrays], core_ids=[0]).results[0]["out"]
```
